# Optimizing a Trainium2 kernel written in Bass

```python
import numpy as np
import jax
import jax.numpy as jnp

def _softmax(x, axis=-1):
    return jax.nn.softmax(x, axis=axis)

def _gelu(x):
    return jax.nn.gelu(x, approximate=True)

def _silu(x):
    return jax.nn.silu(x)

def _sigmoid(x):
    return jax.nn.sigmoid(x)

def _layernorm(x, axis=-1, eps=1e-05):
    m = jnp.mean(x, axis=axis, keepdims=True)
    v = jnp.var(x, axis=axis, keepdims=True)
    return (x - m) / jnp.sqrt(v + eps)

def _scatter_add(tgt, idx, src, axis=0):
    return tgt.at[idx].add(src)

def _segment_sum(src, seg, n):
    return jax.ops.segment_sum(src, seg, n)
kernel_name = 'mk_dlrm_tower_d1_rec_r8_6c358f'

def setup_inputs(seed: int=0):
    np.random.seed(seed)
    _w = jnp.asarray

    def _rec_inputs():
        import jax
        import jax.numpy as jnp
        _tk = jax.random.key(seed)
        ids = jnp.stack([jax.random.randint(jax.random.fold_in(_tk, 200 + f), (512,), 0, v, jnp.int32) for f, v in enumerate([12500, 1000, 1250, 1250, 1000, 1000, 12500, 1250, 125000, 12500, 12500, 1250, 1000, 1250, 1000, 12500, 1000, 12500, 1250, 1250, 12500, 1250, 1250, 12500, 1250, 1000])], axis=1)
        tbl_0 = 0.05 * jax.random.normal(jax.random.fold_in(_tk, 500 + 0), (12500, 128), jnp.float32)
        tbl_1 = 0.05 * jax.random.normal(jax.random.fold_in(_tk, 500 + 1), (1000, 128), jnp.float32)
        tbl_2 = 0.05 * jax.random.normal(jax.random.fold_in(_tk, 500 + 2), (1250, 128), jnp.float32)
        tbl_3 = 0.05 * jax.random.normal(jax.random.fold_in(_tk, 500 + 3), (1250, 128), jnp.float32)
        tbl_4 = 0.05 * jax.random.normal(jax.random.fold_in(_tk, 500 + 4), (1000, 128), jnp.float32)
        tbl_5 = 0.05 * jax.random.normal(jax.random.fold_in(_tk, 500 + 5), (1000, 128), jnp.float32)
        tbl_6 = 0.05 * jax.random.normal(jax.random.fold_in(_tk, 500 + 6), (12500, 128), jnp.float32)
        tbl_7 = 0.05 * jax.random.normal(jax.random.fold_in(_tk, 500 + 7), (1250, 128), jnp.float32)
        tbl_8 = 0.05 * jax.random.normal(jax.random.fold_in(_tk, 500 + 8), (125000, 128), jnp.float32)
        tbl_9 = 0.05 * jax.random.normal(jax.random.fold_in(_tk, 500 + 9), (12500, 128), jnp.float32)
        tbl_10 = 0.05 * jax.random.normal(jax.random.fold_in(_tk, 500 + 10), (12500, 128), jnp.float32)
        tbl_11 = 0.05 * jax.random.normal(jax.random.fold_in(_tk, 500 + 11), (1250, 128), jnp.float32)
        tbl_12 = 0.05 * jax.random.normal(jax.random.fold_in(_tk, 500 + 12), (1000, 128), jnp.float32)
        tbl_13 = 0.05 * jax.random.normal(jax.random.fold_in(_tk, 500 + 13), (1250, 128), jnp.float32)
        tbl_14 = 0.05 * jax.random.normal(jax.random.fold_in(_tk, 500 + 14), (1000, 128), jnp.float32)
        tbl_15 = 0.05 * jax.random.normal(jax.random.fold_in(_tk, 500 + 15), (12500, 128), jnp.float32)
        tbl_16 = 0.05 * jax.random.normal(jax.random.fold_in(_tk, 500 + 16), (1000, 128), jnp.float32)
        tbl_17 = 0.05 * jax.random.normal(jax.random.fold_in(_tk, 500 + 17), (12500, 128), jnp.float32)
        tbl_18 = 0.05 * jax.random.normal(jax.random.fold_in(_tk, 500 + 18), (1250, 128), jnp.float32)
        tbl_19 = 0.05 * jax.random.normal(jax.random.fold_in(_tk, 500 + 19), (1250, 128), jnp.float32)
        tbl_20 = 0.05 * jax.random.normal(jax.random.fold_in(_tk, 500 + 20), (12500, 128), jnp.float32)
        tbl_21 = 0.05 * jax.random.normal(jax.random.fold_in(_tk, 500 + 21), (1250, 128), jnp.float32)
        tbl_22 = 0.05 * jax.random.normal(jax.random.fold_in(_tk, 500 + 22), (1250, 128), jnp.float32)
        tbl_23 = 0.05 * jax.random.normal(jax.random.fold_in(_tk, 500 + 23), (12500, 128), jnp.float32)
        tbl_24 = 0.05 * jax.random.normal(jax.random.fold_in(_tk, 500 + 24), (1250, 128), jnp.float32)
        tbl_25 = 0.05 * jax.random.normal(jax.random.fold_in(_tk, 500 + 25), (1000, 128), jnp.float32)
        _rk = jax.random.fold_in(_tk, 7)
        r_dense_proj = -0.000520686 + 1.00062 * jax.random.normal(jax.random.fold_in(_rk, 101), (512, 128), jnp.float32)
        W_top1 = 0.0405887 * jax.random.normal(jax.random.fold_in(_tk, 801), (607, 512), jnp.float32)
        W_top2 = 0.0441942 * jax.random.normal(jax.random.fold_in(_tk, 802), (512, 256), jnp.float32)
        W_top3 = 0.0625 * jax.random.normal(jax.random.fold_in(_tk, 803), (256, 1), jnp.float32)
        b_top1 = jnp.zeros((512,), jnp.float32)
        b_top2 = jnp.zeros((256,), jnp.float32)
        return (r_dense_proj, ids, tbl_0, tbl_1, tbl_2, tbl_3, tbl_4, tbl_5, tbl_6, tbl_7, tbl_8, tbl_9, tbl_10, tbl_11, tbl_12, tbl_13, tbl_14, tbl_15, tbl_16, tbl_17, tbl_18, tbl_19, tbl_20, tbl_21, tbl_22, tbl_23, tbl_24, tbl_25, W_top1, b_top1, W_top2, b_top2, W_top3)
    r_dense_proj, ids, tbl_0, tbl_1, tbl_2, tbl_3, tbl_4, tbl_5, tbl_6, tbl_7, tbl_8, tbl_9, tbl_10, tbl_11, tbl_12, tbl_13, tbl_14, tbl_15, tbl_16, tbl_17, tbl_18, tbl_19, tbl_20, tbl_21, tbl_22, tbl_23, tbl_24, tbl_25, W_top1, b_top1, W_top2, b_top2, W_top3 = _rec_inputs()

    def _L0_rec_setup():
        import jax, jax.numpy as jnp
        import numpy as np
        key = jax.random.key(seed)
        k1, k2 = jax.random.split(key)
        B, N_SPARSE, D = (2048, 26, 128)
        dense_proj = jax.random.normal(k1, (B, D), dtype=jnp.float32)
        sparse_embs = jax.random.normal(k2, (B, N_SPARSE, D), dtype=jnp.float32)
        return {'dense_proj': dense_proj, 'sparse_embs': sparse_embs}
    _L0_rec_all = _L0_rec_setup()
    _L0_rec_in = {k: v for k, v in _L0_rec_all.items() if k in ()}
    del _L0_rec_all
    return {'r_dense_proj': r_dense_proj, 'ids': ids, 'tbl_0': tbl_0, 'tbl_1': tbl_1, 'tbl_2': tbl_2, 'tbl_3': tbl_3, 'tbl_4': tbl_4, 'tbl_5': tbl_5, 'tbl_6': tbl_6, 'tbl_7': tbl_7, 'tbl_8': tbl_8, 'tbl_9': tbl_9, 'tbl_10': tbl_10, 'tbl_11': tbl_11, 'tbl_12': tbl_12, 'tbl_13': tbl_13, 'tbl_14': tbl_14, 'tbl_15': tbl_15, 'tbl_16': tbl_16, 'tbl_17': tbl_17, 'tbl_18': tbl_18, 'tbl_19': tbl_19, 'tbl_20': tbl_20, 'tbl_21': tbl_21, 'tbl_22': tbl_22, 'tbl_23': tbl_23, 'tbl_24': tbl_24, 'tbl_25': tbl_25, 'W_top1': W_top1, 'b_top1': b_top1, 'W_top2': W_top2, 'b_top2': b_top2, 'W_top3': W_top3}

def reference(r_dense_proj, ids, tbl_0, tbl_1, tbl_2, tbl_3, tbl_4, tbl_5, tbl_6, tbl_7, tbl_8, tbl_9, tbl_10, tbl_11, tbl_12, tbl_13, tbl_14, tbl_15, tbl_16, tbl_17, tbl_18, tbl_19, tbl_20, tbl_21, tbl_22, tbl_23, tbl_24, tbl_25, W_top1, b_top1, W_top2, b_top2, W_top3):
    import jax
    import jax.numpy as jnp

    def _L0_rec_ref(dense_proj, sparse_embs):
        import jax, jax.numpy as jnp
        import numpy as np
        all_vecs = jnp.concatenate([dense_proj[:, None, :], sparse_embs], axis=1)
        n = all_vecs.shape[1]
        interactions = jnp.einsum('bnd,bmd->bnm', all_vecs, all_vecs)
        rows, cols = np.triu_indices(n, k=1)
        interact_flat = interactions[:, rows, cols]
        return jnp.concatenate([dense_proj, interact_flat], axis=1)
    e = jnp.stack([tbl_0[ids[:, 0]], tbl_1[ids[:, 1]], tbl_2[ids[:, 2]], tbl_3[ids[:, 3]], tbl_4[ids[:, 4]], tbl_5[ids[:, 5]], tbl_6[ids[:, 6]], tbl_7[ids[:, 7]], tbl_8[ids[:, 8]], tbl_9[ids[:, 9]], tbl_10[ids[:, 10]], tbl_11[ids[:, 11]], tbl_12[ids[:, 12]], tbl_13[ids[:, 13]], tbl_14[ids[:, 14]], tbl_15[ids[:, 15]], tbl_16[ids[:, 16]], tbl_17[ids[:, 17]], tbl_18[ids[:, 18]], tbl_19[ids[:, 19]], tbl_20[ids[:, 20]], tbl_21[ids[:, 21]], tbl_22[ids[:, 22]], tbl_23[ids[:, 23]], tbl_24[ids[:, 24]], tbl_25[ids[:, 25]]], axis=1)
    z = _L0_rec_ref(r_dense_proj, e)
    z = z.reshape(z.shape[0], -1)
    h = jnp.concatenate([z, r_dense_proj], axis=1)
    h = jnp.maximum(h @ W_top1 + b_top1, 0.0)
    h = jnp.maximum(h @ W_top2 + b_top2, 0.0)
    y = h @ W_top3
    return y

_drawn_inputs = setup_inputs


def setup_inputs(seed=0):
    import zlib

    import numpy as np

    out = dict(_drawn_inputs(seed))
    spreads = {'b_top1': (0.0, 0.1), 'b_top2': (0.0, 0.1)}
    factors = {}
    for name, (base, spread) in spreads.items():
        noise = np.random.default_rng([zlib.crc32(name.encode()), seed]).standard_normal(out[name].shape)
        drawn = base * np.exp(spread * noise) if base else spread * noise
        out[name] = jnp.asarray(drawn.astype(out[name].dtype))
    for name, factor in factors.items():
        out[name] = (out[name] * factor).astype(out[name].dtype)
    return out
```

```python
from contextlib import ExitStack

import concourse.bass as bass
from concourse import mybir
from concourse.alu_op_type import AluOpType as ALU

F32 = mybir.dt.float32
U32 = mybir.dt.uint32
ACT = mybir.ActivationFunctionType
P = 128
Q = 32
NQ = P // Q
BANK = 512
PER_BANK = BANK // P
DMA = 16

RECT_ROWS = (3, 3, 3, 3, 3, 3, 4, 4)


def build(nc, dense, ids, tables, W1, b1, W2, b2, W3, out):
    B, D = dense.shape
    NF = len(tables)
    NV = NF + 1
    T = B // P
    H1, H2 = W2.shape
    C1, C2 = H1 // P, H2 // P
    CH = C1 // 2
    NPAIR = NV * (NV - 1) // 2
    NG = -(-NV // PER_BANK)
    GB = Q // 2
    assert D == P and W1.shape[0] == 2 * D + NPAIR and sum(RECT_ROWS) == NV - 1

    rects = []
    place = 0
    for i, n in enumerate(RECT_ROWS):
        a0 = sum(RECT_ROWS[:i])
        rects.append((a0, a0 + n, place))
        place += n * (NV - a0 - 1)
    NZ = place
    NR = -(-NZ // P)
    assert NR * P <= BANK

    def pair_row(a, n):
        return D + a * NV - a * (a + 1) // 2 + n - a - 1

    w1_runs = []
    for a0, a1, place in rects:
        for a in range(a0, a1):
            k = place + (a - a0) * (NV - a0 - 1) + a - a0
            row, n = pair_row(a, a + 1), NV - 1 - a
            first = min(n, P - k % P)
            w1_runs += [(row, k, first)] + [(row + first, k + first, n - first)] * (n > first)

    with ExitStack() as ctx:
        def sb(name, shape, dt=F32):
            return ctx.enter_context(nc.sbuf_tensor(name, shape, dt))

        def ps(name, shape):
            return ctx.enter_context(nc.psum_tensor(name, shape, F32))

        def sem(name):
            return ctx.enter_context(nc.semaphore(name))

        idx = sb("idx", [P, T, NF], U32)
        dense_sb = sb("dense_sb", [P, T, D])
        emb = sb("emb", [P, NF, D])
        ident = sb("ident", [P, P])
        VT = sb("VT", [P, B, NV])
        denseT = sb("denseT", [P, B])
        Z = sb("Z", [P, NV - 1, Q])
        packed = sb("packed", [P, NR * P])
        ZT = sb("ZT", [P, NR, P])
        h1 = sb("h1", [P, C1, P])
        h2 = sb("h2", [P, C2, P])
        y = sb("y", [1, B])
        w1_dense = sb("w1_dense", [P, 2, H1])
        w1_pair = sb("w1_pair", [P, NR, H1])
        w2 = sb("w2", [P, C1, H2])
        rows = sb("rows", [C1 + 2 * C2, P])
        cols = sb("cols", [P, C1 + 2 * C2])

        turn_ps = ps("turn_ps", [P, 2, PER_BANK, P])
        gram_ps = ps("gram_ps", [P, 2, BANK])
        zt_ps = ps("zt_ps", [P, PER_BANK, P])
        h1_ps = ps("h1_ps", [P, 2, PER_BANK, P])
        h2_own = ps("h2_own", [P, BANK])
        h2_ps = [zt_ps[:, 0, :], h2_own[:, 0:P]]
        y_ps = zt_ps[:, 1, :]

        ids_in = sem("ids_in")
        dense_in = sem("dense_in")
        rows_in = sem("rows_in")
        w1_dense_in = sem("w1_dense_in")
        w1_pair_in = sem("w1_pair_in")
        w2_in = sem("w2_in")
        gathered = [sem(f"gathered{f}") for f in range(NF)]
        ident_zero = sem("ident_zero")
        ident_ready = sem("ident_ready")
        w1_zero = sem("w1_zero")
        psum_zero = sem("psum_zero")
        pad_zero = sem("pad_zero")
        rows_turned = sem("rows_turned")
        cols_ready = sem("cols_ready")
        turned = sem("turned")
        vt_act = sem("vt_act")
        vt_dve = sem("vt_dve")
        denseT_ready = sem("denseT_ready")
        gram_done = sem("gram_done")
        z_ready = sem("z_ready")
        packed_ready = sem("packed_ready")
        zt_done = sem("zt_done")
        zt_copied = sem("zt_copied")
        h1_done = sem("h1_done")
        h1_act = sem("h1_act")
        h1_dve = sem("h1_dve")
        h2_done = sem("h2_done")
        h2_act = sem("h2_act")
        h2_dve = sem("h2_dve")
        y_done = sem("y_done")
        y_ready = sem("y_ready")
        y_out = sem("y_out")

        def group(q):
            return range(q * PER_BANK, min((q + 1) * PER_BANK, NV))

        def copy_vt(eng_copy, t, q):
            v = group(q)
            src = turn_ps[:, (t * NG + q) % 2, 0:len(v), :].rearrange("d v b -> d b v")
            return eng_copy(VT[:, t * P:(t + 1) * P, v[0]:v[-1] + 1], src)

        block = ctx.enter_context(nc.Block())

        @block.sync
        def _(sp):
            sp.dma_start(idx[:], ids.rearrange("(t p) f -> p t f", p=P)).then_inc(ids_in, DMA)
            sp.dma_start(dense_sb[:], dense.rearrange("(t p) d -> p t d", p=P)).then_inc(dense_in, DMA)
            sp.dma_start(w1_dense[:, 0, :], W1[0:D, :]).then_inc(w1_dense_in, DMA)
            sp.dma_start(w1_dense[:, 1, :], W1[D + NPAIR:, :]).then_inc(w1_dense_in, DMA)
            sp.dma_start(w2[:], W2.rearrange("(c p) o -> p c o", p=P)).then_inc(w2_in, DMA)
            sp.wait_ge(w1_zero, 1)
            for row, k, n in w1_runs:
                sp.dma_start(w1_pair[k % P:k % P + n, k // P, :], W1[row:row + n, :]).then_inc(w1_pair_in, DMA)
            for t in range(T):
                sp.wait_ge(y_ready, t + 1)
                sp.dma_start(out[t * P:(t + 1) * P, :].rearrange("b o -> o b"),
                             y[:, t * P:(t + 1) * P]).then_inc(y_out, DMA)
            sp.wait_ge(y_out, DMA * T)

        @block.gpsimd
        def _(pool):
            pool.memset(ident[:], 0.0).then_inc(ident_zero, 1)
            pool.wait_ge(ident_zero, 1)
            pool.affine_select(out=ident[:], in_=ident[:], compare_op=ALU.not_equal, fill=1.0, base=0,
                               pattern=[[-1, P]], channel_multiplier=1).then_inc(ident_ready, 1)
            pool.wait_ge(ids_in, DMA)
            for t in range(T):
                for f in range(NF):
                    if t >= 1:
                        pool.wait_ge(turned, (t - 1) * NG + (f + 1) // PER_BANK + 1)
                    pool.indirect_dma_start(emb[:, f, :], None, tables[f],
                                            bass.IndirectOffsetOnAxis(idx[:, t, f:f + 1], 0)
                                            ).then_inc(gathered[f], DMA)

        @block.tensor
        def _(pe):
            pe.wait_ge(ident_ready, 1)
            pe.wait_ge(rows_in, 3 * DMA)
            pe.transpose(zt_ps[:, 0, 0:C1 + 2 * C2], rows[:], ident[0:C1 + 2 * C2, 0:C1 + 2 * C2]
                         ).then_inc(rows_turned, 1)
            pe.wait_ge(psum_zero, 1)
            for t in range(T):
                for q in range(NG):
                    i = t * NG + q
                    if i >= 2:
                        pe.wait_ge([vt_act, vt_dve][i % 2], i // 2)
                    for v in group(q):
                        if v == 0:
                            pe.wait_ge(dense_in, DMA)
                            rows_of = dense_sb[:, t, :]
                        else:
                            pe.wait_ge(gathered[v - 1], DMA * (t + 1))
                            rows_of = emb[:, v - 1, :]
                        last = pe.transpose(turn_ps[:, i % 2, v % PER_BANK, :], rows_of, ident[:])
                    last.then_inc(turned, 1)
                done = (t + 1) * NG
                pe.wait_ge(vt_act, (done + 1) // 2)
                pe.wait_ge(vt_dve, done // 2)
                if t >= 1:
                    pe.wait_ge(z_ready, t)
                for g in range(Q):
                    for j in range(NQ):
                        v = VT[:, t * P + j * Q + g, :]
                        c = (g % GB) * NV
                        last = pe.matmul(gram_ps[j * Q:j * Q + NV, g // GB, c:c + NV], v, v,
                                         start=True, stop=True, tile_position=(0, j * Q))
                last.then_inc(gram_done, 1)
                if t == 0:
                    pe.wait_ge(w1_dense_in, 2 * DMA)
                pe.wait_ge(denseT_ready, t + 1)
                if t >= 1:
                    pe.wait_ge(h1_act, CH * t)
                    pe.wait_ge(h1_dve, CH * t)
                for o in range(C1):
                    for k in range(2):
                        pe.matmul(h1_ps[:, o // CH, o % CH, :], w1_dense[:, k, o * P:(o + 1) * P], denseT[:, t * P:(t + 1) * P],
                                  start=(o % CH == 0 and k == 0), stop=False, skip_group_check=True)
                pe.wait_ge(packed_ready, t + 1)
                if t == 0:
                    pe.wait_ge(cols_ready, 1)
                    pe.wait_ge(pad_zero, 1)
                else:
                    pe.wait_ge(y_ready, t)
                for r in range(NR):
                    last = pe.transpose(zt_ps[:, r, :], packed[:, r * P:(r + 1) * P], ident[:])
                last.then_inc(zt_done, 1)
                if t == 0:
                    pe.wait_ge(w1_pair_in, DMA * len(w1_runs))
                pe.wait_ge(zt_copied, t + 1)
                for o in range(C1):
                    for r in range(NR):
                        last = pe.matmul(h1_ps[:, o // CH, o % CH, :], w1_pair[:, r, o * P:(o + 1) * P], ZT[:, r, :],
                                         start=False, stop=(r == NR - 1), skip_group_check=True)
                    if o % CH == CH - 1:
                        last.then_inc(h1_done, 1)
                if t == 0:
                    pe.wait_ge(w2_in, DMA)
                else:
                    pe.wait_ge(h2_dve, t)
                for k in range(C1):
                    pe.wait_ge([h1_act, h1_dve][k // CH], CH * t + k % CH + 1)
                    for o in range(C2):
                        last = pe.matmul(h2_ps[o], w2[:, k, o * P:(o + 1) * P], h1[:, k, :],
                                         start=(k == 0), stop=(k == C1 - 1))
                last.then_inc(h2_done, 1)
                for k in range(C2):
                    pe.wait_ge([h2_act, h2_dve][k], t + 1)
                    last = pe.matmul(y_ps[0:1, :], cols[:, C1 + C2 + k:C1 + C2 + k + 1], h2[:, k, :],
                                     start=(k == 0), stop=(k == C2 - 1))
                last.then_inc(y_done, 1)

        @block.scalar
        def _(act):
            act.dma_start(rows[0:C1, :], b1.rearrange("(c p) -> c p", p=P)).then_inc(rows_in, DMA)
            act.dma_start(rows[C1:C1 + C2, :], b2.rearrange("(c p) -> c p", p=P)).then_inc(rows_in, DMA)
            act.dma_start(rows[C1 + C2:, :], W3.rearrange("(c p) o -> c (p o)", p=P)).then_inc(rows_in, DMA)
            for t in range(T):
                for q in range(NG):
                    i = t * NG + q
                    if q == 0:
                        act.wait_ge(turned, i + 1)
                        act.copy(denseT[:, t * P:(t + 1) * P], turn_ps[:, i % 2, 0, :]).then_inc(denseT_ready, 1)
                    if i % 2 == 0:
                        act.wait_ge(turned, i + 1)
                        copy_vt(act.copy, t, q).then_inc(vt_act, 1)
                act.wait_ge(zt_done, t + 1)
                if t >= 1:
                    act.wait_ge(h1_done, 2 * t)
                act.copy(ZT[:], zt_ps[:, 0:NR, :]).then_inc(zt_copied, 1)
                if t == 0:
                    act.wait_ge(cols_ready, 1)
                else:
                    act.wait_ge(h2_done, t)
                act.wait_ge(h1_done, 2 * t + 1)
                for o in range(CH):
                    act.activation(h1[:, o, :], h1_ps[:, 0, o, :], ACT.Relu, bias=cols[:, o:o + 1]).then_inc(h1_act, 1)
                act.wait_ge(h2_done, t + 1)
                if t >= 1:
                    act.wait_ge(y_done, t)
                act.activation(h2[:, 0, :], h2_ps[0], ACT.Relu, bias=cols[:, C1:C1 + 1]).then_inc(h2_act, 1)
                act.wait_ge(y_done, t + 1)
                act.copy(y[:, t * P:(t + 1) * P], y_ps[0:1, :]).then_inc(y_ready, 1)

        @block.vector
        def _(dve):
            dve.memset(gram_ps[:], 0.0).then_inc(psum_zero, 1)
            dve.memset(w1_pair[:], 0.0).then_inc(w1_zero, 1)
            dve.memset(packed[:, NZ:], 0.0).then_inc(pad_zero, 1)
            dve.wait_ge(rows_turned, 1)
            dve.tensor_copy(cols[:], zt_ps[:, 0, 0:C1 + 2 * C2]).then_inc(cols_ready, 1)
            for t in range(T):
                for q in range(NG):
                    i = t * NG + q
                    if i % 2 == 1:
                        dve.wait_ge(turned, i + 1)
                        if q == 0:
                            dve.wait_ge(denseT_ready, t + 1)
                        copy_vt(dve.tensor_copy, t, q).then_inc(vt_dve, 1)
                dve.wait_ge(gram_done, t + 1)
                src = gram_ps[:, :, 0:GB * NV].rearrange("p h (g a) -> p a h g", a=NV)[:, 0:NV - 1]
                dve.transpose(Z[:], src).then_inc(z_ready, 1)
                dve.wait_ge(z_ready, t + 1)
                if t >= 1:
                    dve.wait_ge(zt_done, t)
                for a0, a1, place in rects:
                    w = NV - 1 - a0
                    dst = packed[:, place:place + (a1 - a0) * w].rearrange("p (a n) -> p a n", n=w)
                    last = dve.tensor_copy(dst, Z[:, a0:a1, a0 + 1:NV])
                last.then_inc(packed_ready, 1)
                if t >= 1:
                    dve.wait_ge(h2_done, t)
                dve.wait_ge(h1_done, 2 * t + 2)
                for o in range(CH, C1):
                    dve.tensor_scalar(h1[:, o, :], h1_ps[:, 1, o - CH, :], cols[:, o:o + 1], 0.0, ALU.add, ALU.max
                                      ).then_inc(h1_dve, 1)
                dve.wait_ge(h2_done, t + 1)
                if t >= 1:
                    dve.wait_ge(y_done, t)
                dve.tensor_scalar(h2[:, 1, :], h2_ps[1], cols[:, C1 + 1:C1 + 2], 0.0, ALU.add, ALU.max
                                  ).then_inc(h2_dve, 1)


NF_IN = 26
_INS = ["r_dense_proj", "ids"] + [f"tbl_{f}" for f in range(NF_IN)] + ["W_top1", "b_top1", "W_top2", "b_top2", "W_top3"]


def kernel(**inputs):
    import numpy as np
    import concourse.bacc as bacc
    from concourse.bass_utils import run_bass_kernel_spmd

    nc = bacc.Bacc("TRN2", target_bir_lowering=False, num_devices=1)
    arrays, args = {}, []
    for name in _INS:
        a = np.ascontiguousarray(inputs[name])
        dt = U32 if name == "ids" else mybir.dt.from_np(a.dtype)
        arrays[f"in_{name}"] = a
        args.append(nc.dram_tensor(f"in_{name}", a.shape, dt, kind="ExternalInput").ap())
    B = inputs["ids"].shape[0]
    out = nc.dram_tensor("out_y", (B, 1), F32, kind="ExternalOutput").ap()
    dense, ids, tables, top = args[0], args[1], args[2:2 + NF_IN], args[2 + NF_IN:]
    build(nc, dense, ids, tables, *top, out)
    return run_bass_kernel_spmd(nc, [arrays], core_ids=[0]).results[0]["out_y"]
```

```python
from contextlib import ExitStack

import concourse.bass as bass
from concourse import mybir
from concourse.alu_op_type import AluOpType as ALU

F32 = mybir.dt.float32
BF16 = mybir.dt.bfloat16
F16 = mybir.dt.float16
U32 = mybir.dt.uint32
ACT = mybir.ActivationFunctionType
P = 128
Q = 32
NQ = P // Q
BANK = 512
PER_BANK = BANK // P
DMA = 16

HOT = (1, 4, 5, 12, 14, 25)
HOT_ROWS_MAX = 2048
HOT_P = 125

RECT_ROWS = (3, 3, 3, 3, 3, 3, 4, 4)


def build(nc, dense, ids, tables, W1, b1, W2, b2, W3, out):
    B, D = dense.shape
    NF = len(tables)
    NV = NF + 1
    T = B // P
    H1, H2 = W2.shape
    C1, C2 = H1 // P, H2 // P
    CH = C1 // 2
    NPAIR = NV * (NV - 1) // 2
    GB = Q // 2
    assert D == P and W1.shape[0] == 2 * D + NPAIR and sum(RECT_ROWS) == NV - 1 and B == BANK

    NH = len(HOT)
    HK = tables[HOT[0]].shape[0] // HOT_P
    assert all(tables[f].shape[0] == HK * HOT_P <= HOT_ROWS_MAX for f in HOT)

    turned_v = [v for v in range(NV) if v - 1 not in HOT]
    groups = [turned_v[i:i + PER_BANK] for i in range(0, len(turned_v), PER_BANK)]
    NG = len(groups)
    assert NG % 2 == 0 and NG >= NH
    group_of = {v: q for q, vs in enumerate(groups) for v in vs}

    def runs(vs):
        found = []
        for i, v in enumerate(vs):
            if found and found[-1][1] + found[-1][2] == v:
                found[-1][2] += 1
            else:
                found.append([i, v, 1])
        return found

    rects = []
    place = 0
    for i, n in enumerate(RECT_ROWS):
        a0 = sum(RECT_ROWS[:i])
        rects.append((a0, a0 + n, place))
        place += n * (NV - a0 - 1)
    NZ = place
    NR = -(-NZ // P)
    assert NR < PER_BANK
    ends = [next((i + 1 for i, x in enumerate(rects[1:]) if x[2] >= (r + 1) * P), len(rects)) for r in range(NR)]
    rects_of = [rects[0 if r == 0 else ends[r - 1]:ends[r]] for r in range(NR)]

    steps = [[(t, range(NR))] for t in range(T - 1)] + [[(T - 1 + r, (r,)) for r in range(NR)]]

    w1_runs = []
    row = D
    for a0, a1, place in rects:
        for a in range(a0, a1):
            k = place + (a - a0) * (NV - a0 - 1) + a - a0
            n = NV - 1 - a
            first = min(n, P - k % P)
            w1_runs += [(row, k, first)] + [(row + first, k + first, n - first)] * (n > first)
            row += n

    with ExitStack() as ctx:
        def sb(name, shape, dt=F32):
            return ctx.enter_context(nc.sbuf_tensor(name, shape, dt))

        def ps(name, shape):
            return ctx.enter_context(nc.psum_tensor(name, shape, F32))

        def sem(name):
            return ctx.enter_context(nc.semaphore(name))

        idx = sb("idx", [P, T, NF], U32)
        hot_ids = sb("hot_ids", [P, NH, T], F16)
        row_of = sb("row_of", [P, HK])
        ids_all = sb("ids_all", [P, 2, B], F16)
        onehot = sb("onehot", [P, 2, HK, B], BF16)
        hot_tab = sb("hot_tab", [HOT_P, NH, HK * D])
        rest = sb("rest", [HOT_P, 2, HK * D])
        low = sb("low", [HOT_P, 2, HK * D], BF16)
        dense_sb = sb("dense_sb", [P, T, D])
        emb = sb("emb", [P, NF, D])
        ident = sb("ident", [P, P])
        ident16 = sb("ident16", [P, P], F16)
        VT = sb("VT", [P, B, NV])
        denseT = sb("denseT", [P, B])
        Z = sb("Z", [P, NV - 1, Q])
        packed = sb("packed", [P, NR * P])
        ZT = sb("ZT", [P, NR, P])
        h1 = sb("h1", [P, C1, P])
        h2 = sb("h2", [P, C2, P])
        y = sb("y", [1, B])
        w1_dense = sb("w1_dense", [P, 2, H1])
        w1_sum = sb("w1_sum", [P, H1])
        w1_pair = sb("w1_pair", [P, NR, H1])
        w2 = sb("w2", [P, C1, H2])
        rows = sb("rows", [C1 + 2 * C2, P])
        cols = sb("cols", [P, C1 + 2 * C2])

        turn_ps = ps("turn_ps", [P, 2, PER_BANK, P])
        gram_ps = ps("gram_ps", [P, 2, BANK])
        h1_ps = ps("h1_ps", [P, 2, PER_BANK, P])
        zt_ps = ps("zt_ps", [P, PER_BANK, P])
        h2_own = ps("h2_own", [P, PER_BANK, P])
        hot_ps = h1_ps
        ids_ps = h2_own
        h2_ps = [zt_ps[:, 0], h2_own[:, 0]]
        y_ps = zt_ps[0:1, 1]
        last_zt = [zt_ps[:, 0], turn_ps[:, 0, 0], turn_ps[:, 1, 0]]

        ids_in = sem("ids_in")
        hot_in = [sem(f"hot_in{h}") for h in range(NH)]
        dense_in = sem("dense_in")
        rows_in = sem("rows_in")
        w1_dense_in = sem("w1_dense_in")
        w1_pair_in = sem("w1_pair_in")
        w2_in = sem("w2_in")
        gathered = [sem(f"gathered{f}") for f in range(NF)]
        ident_zero = sem("ident_zero")
        ident_ready = sem("ident_ready")
        ident16_ready = sem("ident16_ready")
        row_of_ready = sem("row_of_ready")
        w1_zero = sem("w1_zero")
        psum_zero = sem("psum_zero")
        pad_zero = sem("pad_zero")
        rows_turned = sem("rows_turned")
        cols_ready = sem("cols_ready")
        w1_sum_ready = sem("w1_sum_ready")
        hot_ids_ready = sem("hot_ids_ready")
        ids_spread = sem("ids_spread")
        ids_copied = sem("ids_copied")
        onehot_ready = sem("onehot_ready")
        rest_ready = sem("rest_ready")
        low_ready = sem("low_ready")
        picked = sem("picked")
        vt_hot = sem("vt_hot")
        turned = sem("turned")
        vt_act = sem("vt_act")
        vt_dve = sem("vt_dve")
        denseT_ready = sem("denseT_ready")
        gram_done = sem("gram_done")
        z_ready = sem("z_ready")
        packed_ready = sem("packed_ready")
        zt_done = sem("zt_done")
        zt_copied = sem("zt_copied")
        h1_done = sem("h1_done")
        h1_act = sem("h1_act")
        h1_dve = sem("h1_dve")
        h2_done = sem("h2_done")
        h2_act = sem("h2_act")
        h2_dve = sem("h2_dve")
        y_done = sem("y_done")
        y_ready = sem("y_ready")
        y_out = sem("y_out")

        def high(words, k):
            return words.bitcast(BF16)[:, 2 * k * D + 1:2 * (k + 1) * D:2]

        def vt_copies(copy, t, q):
            for i, v, n in runs(groups[q]):
                src = turn_ps[:, q % 2, i:i + n, :].rearrange("d v b -> d b v")
                last = copy(VT[:, t * P:(t + 1) * P, v:v + n], src)
            return last

        block = ctx.enter_context(nc.Block())

        @block.sync
        def _(sp):
            sp.dma_start(idx[:], ids.rearrange("(t p) f -> p t f", p=P)).then_inc(ids_in, DMA)
            for h, f in enumerate(HOT):
                sp.dma_start(hot_tab[:, h, :], tables[f].rearrange("(p k) d -> p (k d)", p=HOT_P)
                             ).then_inc(hot_in[h], DMA)
            sp.wait_ge(w1_zero, 1)
            for row, k, n in w1_runs:
                sp.dma_start(w1_pair[k % P:k % P + n, k // P, :], W1[row:row + n, :]).then_inc(w1_pair_in, DMA)
            for t in range(T):
                s = slice(t * P, (t + 1) * P)
                sp.wait_ge(y_ready, t + 1)
                sp.dma_start(out[s, :].rearrange("b o -> o b"), y[:, s]).then_inc(y_out, DMA)
            sp.wait_ge(y_out, DMA * T)

        @block.gpsimd
        def _(pool):
            pool.memset(ident[:], 0.0).then_inc(ident_zero, 1)
            pool.wait_ge(ident_zero, 1)
            pool.affine_select(out=ident[:], in_=ident[:], compare_op=ALU.not_equal, fill=1.0, base=0,
                               pattern=[[-1, P]], channel_multiplier=1).then_inc(ident_ready, 1)
            pool.iota(row_of[:], [[1, HK]], base=0, channel_multiplier=HK,
                      allow_small_or_imprecise_dtypes=True).then_inc(row_of_ready, 1)
            pool.memset(w1_pair[:], 0.0).then_inc(w1_zero, 1)
            pool.wait_ge(ids_in, DMA)
            for t in range(T):
                for v in turned_v[1:]:
                    f = v - 1
                    if t >= 1:
                        pool.wait_ge(turned, (t - 1) * NG + group_of[v] + 1)
                    pool.indirect_dma_start(emb[:, f, :], None, tables[f],
                                            bass.IndirectOffsetOnAxis(idx[:, t, f:f + 1], 0)
                                            ).then_inc(gathered[f], DMA)

        @block.tensor
        def _(pe):
            def spread_ids(h):
                if h == 0:
                    pe.wait_ge(hot_ids_ready, 1)
                    pe.wait_ge(ident16_ready, 1)
                else:
                    pe.wait_ge(ids_copied, h)
                for t in range(T):
                    last = pe.matmul(ids_ps[:, t, :], hot_ids[:, h, t:t + 1].to_broadcast([P, P]), ident16[:],
                                     start=True, stop=True)
                last.then_inc(ids_spread, 1)

            def pick(h):
                pe.wait_ge(hot_in[h], DMA)
                if h >= 2:
                    pe.wait_ge(vt_hot, h - 1)
                acc = hot_ps[:, h % 2].rearrange("d t b -> d (t b)")
                for part in range(3):
                    if part == 1:
                        pe.wait_ge(rest_ready, h + 1)
                    if part == 2:
                        pe.wait_ge(low_ready, h + 1)
                    for k in range(HK):
                        w = [high(hot_tab[:, h, :], k), high(rest[:, h % 2, :], k),
                             low[:, h % 2, k * D:(k + 1) * D]][part]
                        if part == 0:
                            pe.wait_ge(onehot_ready, h * HK + k + 1)
                        last = pe.matmul(acc, w, onehot[0:HOT_P, h % 2, k, :],
                                         start=(part == 0 and k == 0), stop=(part == 2 and k == HK - 1))
                last.then_inc(picked, 1)

            def turn(t, q):
                i = t * NG + q
                if i >= 2:
                    pe.wait_ge([vt_act, vt_dve][q % 2], i // 2)
                for at, v in enumerate(groups[q]):
                    if v == 0:
                        pe.wait_ge(dense_in, DMA)
                        rows_of = dense_sb[:, t, :]
                    else:
                        pe.wait_ge(gathered[v - 1], DMA * (t + 1))
                        rows_of = emb[:, v - 1, :]
                    last = pe.transpose(turn_ps[:, q % 2, at, :], rows_of, ident[:])
                last.then_inc(turned, 1)

            def gram(t):
                if t == 0:
                    pe.wait_ge(vt_hot, NH)
                    pe.wait_ge(psum_zero, 1)
                else:
                    pe.wait_ge(z_ready, NR * t)
                pe.wait_ge(vt_act, (t + 1) * NG // 2)
                pe.wait_ge(vt_dve, (t + 1) * NG // 2)
                for g in range(Q):
                    for j in range(NQ):
                        v = VT[:, t * P + j * Q + g, :]
                        c = (g % GB) * NV
                        last = pe.matmul(gram_ps[j * Q:j * Q + NV, g // GB, c:c + NV], v, v,
                                         start=True, stop=True, tile_position=(0, j * Q))
                last.then_inc(gram_done, 1)

            def layer1_dense(t):
                if t == 0:
                    pe.wait_ge(w1_sum_ready, 1)
                    pe.wait_ge(vt_hot, NH)
                else:
                    pe.wait_ge(h1_act, CH * t)
                    pe.wait_ge(h1_dve, CH * t)
                pe.wait_ge(denseT_ready, t + 1)
                for o in range(C1):
                    pe.matmul(h1_ps[:, o // CH, o % CH, :], w1_sum[:, o * P:(o + 1) * P],
                              denseT[:, t * P:(t + 1) * P], start=(o % CH == 0), stop=False, skip_group_check=True)

            def turn_pairs(t, step, chunks):
                pe.wait_ge(packed_ready, NR * t + chunks[-1] + 1)
                if t == 0:
                    pe.wait_ge(cols_ready, 1)
                    pe.wait_ge(pad_zero, 1)
                else:
                    pe.wait_ge(y_ready, t)
                for r in chunks:
                    last = pe.transpose(last_zt[r] if t == T - 1 else zt_ps[:, r, :],
                                        packed[:, r * P:(r + 1) * P], ident[:])
                last.then_inc(zt_done, 1)

            def layer1_pairs(t, step, chunks):
                if t == 0:
                    pe.wait_ge(w1_pair_in, DMA * len(w1_runs))
                pe.wait_ge(zt_copied, step + 1)
                for r in chunks:
                    for o in range(C1):
                        last = pe.matmul(h1_ps[:, o // CH, o % CH, :], w1_pair[:, r, o * P:(o + 1) * P], ZT[:, r, :],
                                         start=False, stop=(r == NR - 1), skip_group_check=True)
                        if r == NR - 1 and o % CH == CH - 1:
                            last.then_inc(h1_done, 1)

            def layer2(t):
                if t == 0:
                    pe.wait_ge(w2_in, DMA)
                else:
                    pe.wait_ge(h2_dve, t)
                for k in range(C1):
                    pe.wait_ge([h1_act, h1_dve][k // CH], CH * t + k % CH + 1)
                    for o in range(C2):
                        last = pe.matmul(h2_ps[o], w2[:, k, o * P:(o + 1) * P], h1[:, k, :],
                                         start=(k == 0), stop=(k == C1 - 1))
                last.then_inc(h2_done, 1)

            def layer3(t):
                for k in range(C2):
                    pe.wait_ge([h2_act, h2_dve][k], t + 1)
                    last = pe.matmul(y_ps, cols[:, C1 + C2 + k:C1 + C2 + k + 1], h2[:, k, :],
                                     start=(k == 0), stop=(k == C2 - 1))
                last.then_inc(y_done, 1)

            pe.wait_ge(ident_ready, 1)
            spread_ids(0)
            for h in range(NH):
                if h + 1 < NH:
                    spread_ids(h + 1)
                pick(h)
                turn(0, h)
                if h == 0:
                    pe.wait_ge(rows_in, 3 * DMA)
                    pe.transpose(zt_ps[:, 0, 0:C1 + 2 * C2], rows[:], ident[0:C1 + 2 * C2, 0:C1 + 2 * C2]
                                 ).then_inc(rows_turned, 1)
            for q in range(NH, NG):
                turn(0, q)
            for t in range(T - 1):
                (pairs,) = steps[t]
                gram(t)
                turn(t + 1, 0)
                layer1_dense(t)
                turn(t + 1, 1)
                turn_pairs(t, *pairs)
                turn(t + 1, 2)
                layer1_pairs(t, *pairs)
                turn(t + 1, 3)
                layer2(t)
                turn(t + 1, 4)
                layer3(t)
                for q in range(5, NG - (t == T - 2)):
                    turn(t + 1, q)
            t = T - 1
            layer1_dense(t)
            turn(t, NG - 1)
            gram(t)
            turn_pairs(t, *steps[t][0])
            for now, then in zip(steps[t], steps[t][1:]):
                layer1_pairs(t, *now)
                turn_pairs(t, *then)
            layer1_pairs(t, *steps[t][-1])
            layer2(t)
            layer3(t)

        @block.scalar
        def _(act):
            def copy_ids(h):
                act.wait_ge(ids_spread, h + 1)
                if h >= 2:
                    act.wait_ge(onehot_ready, (h - 1) * HK)
                act.copy(ids_all[:, h % 2, :], ids_ps[:].rearrange("p t b -> p (t b)")).then_inc(ids_copied, 1)

            def copy_picked(h):
                act.wait_ge(picked, h + 1)
                act.copy(VT[:, :, HOT[h] + 1], hot_ps[:, h % 2].rearrange("d t b -> d (t b)")).then_inc(vt_hot, 1)

            def copy_turned(t, q):
                act.wait_ge(turned, t * NG + q + 1)
                if q == 0:
                    act.copy(denseT[:, t * P:(t + 1) * P], turn_ps[:, 0, 0, :]).then_inc(denseT_ready, 1)
                vt_copies(act.copy, t, q).then_inc(vt_act, 1)

            def copy_pairs(t, step, chunks):
                act.wait_ge(zt_done, step + 1)
                if t >= 1:
                    act.wait_ge(h1_done, 2 * t)
                if t < T - 1:
                    act.copy(ZT[:], zt_ps[:, 0:NR, :]).then_inc(zt_copied, 1)
                else:
                    act.copy(ZT[:, chunks[0], :], last_zt[chunks[0]]).then_inc(zt_copied, 1)

            def relu1(t):
                act.wait_ge(h1_done, 2 * t + 1)
                if t == 0:
                    act.wait_ge(cols_ready, 1)
                else:
                    act.wait_ge(h2_done, t)
                for o in range(CH):
                    act.activation(h1[:, o, :], h1_ps[:, 0, o, :], ACT.Relu, bias=cols[:, o:o + 1]
                                   ).then_inc(h1_act, 1)

            def relu2(t):
                act.wait_ge(h2_done, t + 1)
                if t >= 1:
                    act.wait_ge(y_done, t)
                act.activation(h2[:, 0, :], h2_ps[0], ACT.Relu, bias=cols[:, C1:C1 + 1]).then_inc(h2_act, 1)

            def copy_y(t):
                act.wait_ge(y_done, t + 1)
                act.copy(y[:, t * P:(t + 1) * P], y_ps).then_inc(y_ready, 1)

            act.dma_start(dense_sb[:], dense.rearrange("(t p) d -> p t d", p=P)).then_inc(dense_in, DMA)
            act.dma_start(rows[0:C1, :], b1.rearrange("(c p) -> c p", p=P)).then_inc(rows_in, DMA)
            act.dma_start(rows[C1:C1 + C2, :], b2.rearrange("(c p) -> c p", p=P)).then_inc(rows_in, DMA)
            act.dma_start(rows[C1 + C2:, :], W3.rearrange("(c p) o -> c (p o)", p=P)).then_inc(rows_in, DMA)
            copy_ids(0)
            for h in range(NH):
                if h + 1 < NH:
                    copy_ids(h + 1)
                if h == 1:
                    act.dma_start(w1_dense[:, 0, :], W1[0:D, :]).then_inc(w1_dense_in, DMA)
                    act.dma_start(w1_dense[:, 1, :], W1[D + NPAIR:, :]).then_inc(w1_dense_in, DMA)
                    act.dma_start(w2[:], W2.rearrange("(c p) o -> p c o", p=P)).then_inc(w2_in, DMA)
                copy_picked(h)
                if h % 2 == 0:
                    copy_turned(0, h)
            for q in range(NH + NH % 2, NG, 2):
                copy_turned(0, q)
            for t in range(T - 1):
                copy_turned(t + 1, 0)
                copy_pairs(t, *steps[t][0])
                copy_turned(t + 1, 2)
                relu1(t)
                relu2(t)
                copy_turned(t + 1, 4)
                copy_y(t)
                for q in range(6, NG, 2):
                    copy_turned(t + 1, q)
            t = T - 1
            for step in steps[t]:
                copy_pairs(t, *step)
            relu1(t)
            relu2(t)
            copy_y(t)

        @block.vector
        def _(dve):
            def split(h):
                if h >= 2:
                    dve.wait_ge(picked, h - 1)
                dve.wait_ge(ids_copied, h + 1)
                for k in range(HK):
                    dve.tensor_scalar(onehot[:, h % 2, k, :], ids_all[:, h % 2, :], row_of[:, k:k + 1], None,
                                      ALU.is_equal).then_inc(onehot_ready, 1)
                dve.wait_ge(hot_in[h], DMA)
                words = hot_tab[:, h, :]
                dve.tensor_tensor(rest[:, h % 2, :], words, words.bitcast(BF16)[:, 1::2], ALU.subtract
                                  ).then_inc(rest_ready, 1)
                dve.wait_ge(rest_ready, h + 1)
                words = rest[:, h % 2, :]
                dve.tensor_tensor(low[:, h % 2, :], words, words.bitcast(BF16)[:, 1::2], ALU.subtract
                                  ).then_inc(low_ready, 1)

            def copy_turned(t, q):
                dve.wait_ge(turned, t * NG + q + 1)
                vt_copies(dve.tensor_copy, t, q).then_inc(vt_dve, 1)

            def square(t):
                dve.wait_ge(gram_done, t + 1)
                src = gram_ps[:, :, 0:GB * NV].rearrange("p h (g a) -> p a h g", a=NV)
                for r in range(NR):
                    a0, a1 = rects_of[r][0][0], rects_of[r][-1][1]
                    dve.transpose(Z[:, a0:a1, :], src[:, a0:a1]).then_inc(z_ready, 1)
                    dve.wait_ge(z_ready, NR * t + r + 1)
                    if t >= 1:
                        dve.wait_ge(zt_done, t)
                    for a0, a1, place in rects_of[r]:
                        w = NV - 1 - a0
                        dst = packed[:, place:place + (a1 - a0) * w].rearrange("p (a n) -> p a n", n=w)
                        last = dve.tensor_copy(dst, Z[:, a0:a1, a0 + 1:NV])
                    last.then_inc(packed_ready, 1)

            def relu1(t):
                if t >= 1:
                    dve.wait_ge(h2_done, t)
                dve.wait_ge(h1_done, 2 * t + 2)
                for o in range(CH, C1):
                    dve.tensor_scalar(h1[:, o, :], h1_ps[:, 1, o - CH, :], cols[:, o:o + 1], 0.0, ALU.add, ALU.max
                                      ).then_inc(h1_dve, 1)

            def relu2(t):
                dve.wait_ge(h2_done, t + 1)
                if t >= 1:
                    dve.wait_ge(y_done, t)
                dve.tensor_scalar(h2[:, 1, :], h2_ps[1], cols[:, C1 + 1:C1 + 2], 0.0, ALU.add, ALU.max
                                  ).then_inc(h2_dve, 1)

            dve.memset(gram_ps[:], 0.0).then_inc(psum_zero, 1)
            dve.memset(packed[:, NZ:], 0.0).then_inc(pad_zero, 1)
            dve.wait_ge(ident_ready, 1)
            dve.tensor_copy(ident16[:], ident[:]).then_inc(ident16_ready, 1)
            dve.wait_ge(ids_in, DMA)
            for h, f in enumerate(HOT):
                last = dve.tensor_copy(hot_ids[:, h, :], idx[:, :, f])
            last.then_inc(hot_ids_ready, 1)
            dve.wait_ge(row_of_ready, 1)
            for h in range(NH):
                split(h)
                if h >= 1 and h % 2 == 0:
                    copy_turned(0, h - 1)
                if h == 2:
                    dve.wait_ge(rows_turned, 1)
                    dve.tensor_copy(cols[:], zt_ps[:, 0, 0:C1 + 2 * C2]).then_inc(cols_ready, 1)
            for q in range(NH - 1 | 1, NG, 2):
                copy_turned(0, q)
            dve.wait_ge(w1_dense_in, 2 * DMA)
            dve.tensor_tensor(w1_sum[:], w1_dense[:, 0, :], w1_dense[:, 1, :], ALU.add).then_inc(w1_sum_ready, 1)
            for t in range(T - 1):
                square(t)
                copy_turned(t + 1, 1)
                relu1(t)
                copy_turned(t + 1, 3)
                relu2(t)
                for q in range(5, NG, 2):
                    copy_turned(t + 1, q)
            t = T - 1
            square(t)
            relu1(t)
            relu2(t)


NF_IN = 26
_INS = ["r_dense_proj", "ids"] + [f"tbl_{f}" for f in range(NF_IN)] + ["W_top1", "b_top1", "W_top2", "b_top2", "W_top3"]


def kernel(**inputs):
    import numpy as np
    import concourse.bacc as bacc
    from concourse.bass_utils import run_bass_kernel_spmd

    nc = bacc.Bacc("TRN2", target_bir_lowering=False, num_devices=1)
    arrays, args = {}, []
    for name in _INS:
        a = np.ascontiguousarray(inputs[name])
        dt = U32 if name == "ids" else mybir.dt.from_np(a.dtype)
        arrays[f"in_{name}"] = a
        args.append(nc.dram_tensor(f"in_{name}", a.shape, dt, kind="ExternalInput").ap())
    B = inputs["ids"].shape[0]
    out = nc.dram_tensor("out_y", (B, 1), F32, kind="ExternalOutput").ap()
    dense, ids, tables, top = args[0], args[1], args[2:2 + NF_IN], args[2 + NF_IN:]
    build(nc, dense, ids, tables, *top, out)
    return run_bass_kernel_spmd(nc, [arrays], core_ids=[0]).results[0]["out_y"]
```

```python
from contextlib import ExitStack

import concourse.bass as bass
from concourse import mybir
from concourse.alu_op_type import AluOpType as ALU

F32 = mybir.dt.float32
F16 = mybir.dt.float16
F32R = mybir.dt.float32r
U32 = mybir.dt.uint32
ACT = mybir.ActivationFunctionType
P = 128
Q = 32
NQ = P // Q
BANK = 512
PER_BANK = BANK // P
BUSY_TURN = 2
BUSY_SQUARE = 4
TABS = 4
DMA = 16

HOT = (1, 4, 5, 12, 14, 16, 25)
LATE = 2
LATE_TILES = 3
HOT_ROWS_MAX = 2048
HOT_P = 125

RECT_ROWS = (3, 3, 3, 3, 3, 3, 4, 4)


def build(nc, dense, ids, tables, W1, b1, W2, b2, W3, out):
    B, D = dense.shape
    NF = len(tables)
    NV = NF + 1
    T = B // P
    H1, H2 = W2.shape
    C1, C2 = H1 // P, H2 // P
    CH = C1 // 2
    NPAIR = NV * (NV - 1) // 2
    GB = Q // 2
    assert D == P and W1.shape[0] == 2 * D + NPAIR and sum(RECT_ROWS) == NV - 1 and B == BANK

    NH = len(HOT)
    HK = tables[HOT[0]].shape[0] // HOT_P
    LK = tables[LATE].shape[0] // HOT_P
    rows_on = [HK] * NH + [LK]
    assert all(tables[f].shape[0] == n * HOT_P <= HOT_ROWS_MAX for f, n in zip(HOT + (LATE,), rows_on))

    turned_v = [v for v in range(NV) if v - 1 not in HOT]
    groups = [turned_v[i:min(i + PER_BANK, len(turned_v) - 1)] for i in range(0, len(turned_v) - 1, PER_BANK)]
    groups.append(turned_v[-1:])
    NG = len(groups)
    assert NG == 6 and NG >= NH - 1
    TL = T - LATE_TILES
    late = slice(TL * P, B)
    groups_at = [groups] * TL + [[[v for v in vs if v != LATE + 1] for vs in groups]] * LATE_TILES
    group_of = {v: q for q, vs in enumerate(groups) for v in vs}

    def runs(vs):
        found = []
        for i, v in enumerate(vs):
            if found and found[-1][1] + found[-1][2] == v:
                found[-1][2] += 1
            else:
                found.append([i, v, 1])
        return found

    rects = []
    place = 0
    for i, n in enumerate(RECT_ROWS):
        a0 = sum(RECT_ROWS[:i])
        rects.append((a0, a0 + n, place))
        place += n * (NV - a0 - 1)
    NZ = place
    NR = -(-NZ // P)
    assert NR == 3
    ends = [next((i + 1 for i, x in enumerate(rects[1:]) if x[2] >= (r + 1) * P), len(rects)) for r in range(NR)]
    rects_of = [rects[0 if r == 0 else ends[r - 1]:ends[r]] for r in range(NR)]

    w1_runs = []
    row = D
    for a0, a1, place in rects:
        for a in range(a0, a1):
            k = place + (a - a0) * (NV - a0 - 1) + a - a0
            n = NV - 1 - a
            first = min(n, P - k % P)
            w1_runs += [(row, k, first)] + [(row + first, k + first, n - first)] * (n > first)
            row += n

    with ExitStack() as ctx:
        def sb(name, shape, dt=F32):
            return ctx.enter_context(nc.sbuf_tensor(name, shape, dt))

        def ps(name, shape):
            return ctx.enter_context(nc.psum_tensor(name, shape, F32))

        def sem(name):
            return ctx.enter_context(nc.semaphore(name))

        idx = sb("idx", [P, T, NF], U32)
        hot_ids = sb("hot_ids", [P, NH + 1, T], F16)
        warm_up = sb("warm_up", [P, 1])
        minus_row = sb("minus_row", [P, 2])
        ids_all = sb("ids_all", [P, 2, B], F16)
        onehot = sb("onehot", [P, 2, HK, B], F32R)
        late_onehot = sb("late_onehot", [P, LK, LATE_TILES * P], F32R)
        hot_tab = sb("hot_tab", [HOT_P, TABS, max(HK, LK) * D])
        high = sb("high", [HOT_P, 2, max(HK, LK) * D], F32R)
        low = sb("low", [HOT_P, 2, max(HK, LK) * D], F32R)
        dense_sb = sb("dense_sb", [P, T, D])
        emb = sb("emb", [P, 2, NF, D])
        ident = sb("ident", [P, P])
        ident16 = sb("ident16", [P, P], F16)
        VT = sb("VT", [P, B, NV])
        denseT = sb("denseT", [P, B])
        Z = sb("Z", [P, NV - 1, Q])
        packed = sb("packed", [P, NR * P])
        ZT = sb("ZT", [P, NR, P])
        h1 = sb("h1", [P, C1, P])
        h2 = sb("h2", [P, C2, P])
        y = sb("y", [1, B])
        w1_dense = sb("w1_dense", [P, 2, H1])
        w1_sum = sb("w1_sum", [P, H1])
        w1_pair = sb("w1_pair", [P, NR, H1])
        w2 = sb("w2", [P, C1, H2])
        rows = sb("rows", [C1 + 2 * C2, P])
        cols = sb("cols", [P, C1 + 2 * C2])

        turn_ps = ps("turn_ps", [P, 2, PER_BANK, P])
        gram_ps = ps("gram_ps", [P, 2, BANK])
        h1_ps = ps("h1_ps", [P, 2, PER_BANK, P])
        zt_ps = ps("zt_ps", [P, PER_BANK, P])
        h2_own = ps("h2_own", [P, PER_BANK, P])
        hot_ps = h1_ps
        late_ps = h2_own[:, PER_BANK - LATE_TILES:, :].rearrange("d t b -> d (t b)")
        ids_ps = h2_own
        h2_ps = [zt_ps[:, 0], h2_own[:, 0]]
        y_ps = zt_ps[0:1, 1]
        chunk_ps = [zt_ps[:, 0], h2_own[:, 0], zt_ps[:, 2]]

        first_ids_in = sem("first_ids_in")
        other_ids_in = sem("other_ids_in")
        hot_in = [sem(f"hot_in{h}") for h in range(NH + 1)]
        dense_in = sem("dense_in")
        rows_in = sem("rows_in")
        w1_dense_in = sem("w1_dense_in")
        w1_pair_in = sem("w1_pair_in")
        w2_in = sem("w2_in")
        gathered = [[sem(f"gathered{i}_{f}") for f in range(NF)] for i in range(2)]
        ident_zero = sem("ident_zero")
        ident_ready = sem("ident_ready")
        ident16_ready = sem("ident16_ready")
        minus_row_ready = sem("minus_row_ready")
        w1_zero = sem("w1_zero")
        psum_zero = sem("psum_zero")
        pad_zero = sem("pad_zero")
        rows_turned = sem("rows_turned")
        cols_ready = sem("cols_ready")
        w1_sum_ready = sem("w1_sum_ready")
        hot_ids_ready = sem("hot_ids_ready")
        ids_spread = sem("ids_spread")
        ids_copied = sem("ids_copied")
        onehot_ready = sem("onehot_ready")
        first_high_ready = sem("first_high_ready")
        high_ready = sem("high_ready")
        low_ready = sem("low_ready")
        picked = sem("picked")
        late_onehot_ready = sem("late_onehot_ready")
        late_picked = sem("late_picked")
        vt_late = sem("vt_late")
        vt_hot = sem("vt_hot")
        turned = sem("turned")
        vt_act = sem("vt_act")
        vt_dve = sem("vt_dve")
        denseT_ready = sem("denseT_ready")
        gram_done = sem("gram_done")
        z_ready = sem("z_ready")
        packed_ready = sem("packed_ready")
        zt_done = sem("zt_done")
        zt_copied = sem("zt_copied")
        h1_done = sem("h1_done")
        h1_act = sem("h1_act")
        h1_dve = sem("h1_dve")
        h2_done = sem("h2_done")
        h2_act = sem("h2_act")
        h2_dve = sem("h2_dve")
        y_done = sem("y_done")
        y_ready = sem("y_ready")
        y_out = sem("y_out")

        def wait_high(eng, h):
            if h == 0:
                eng.wait_ge(first_high_ready, 1)
            else:
                eng.wait_ge(high_ready, h)

        def vt_copies(copy, t, q):
            for i, v, n in runs(groups_at[t][q]):
                src = turn_ps[:, q % 2, i:i + n, :].rearrange("d v b -> d b v")
                last = copy(VT[:, t * P:(t + 1) * P, v:v + n], src)
            return last

        block = ctx.enter_context(nc.Block())

        @block.sync
        def _(sp):
            sp.dma_start(idx[:, 0, :], ids[0:P, :]).then_inc(first_ids_in, DMA)
            sp.dma_start(idx[:, 1:, :], ids[P:, :].rearrange("(t p) f -> p t f", p=P)).then_inc(other_ids_in, DMA)
            for h, f in enumerate(HOT + (LATE,)):
                if h >= TABS:
                    sp.wait_ge(low_ready, h - TABS + 1)
                sp.dma_start(hot_tab[:, h % TABS, 0:rows_on[h] * D], tables[f].rearrange("(p k) d -> p (k d)", p=HOT_P)
                             ).then_inc(hot_in[h], DMA)
                if h == 0:
                    sp.dma_start(dense_sb[:], dense.rearrange("(t p) d -> p t d", p=P)).then_inc(dense_in, DMA)
                    sp.dma_start(rows[0:C1, :], b1.rearrange("(c p) -> c p", p=P)).then_inc(rows_in, DMA)
                    sp.dma_start(rows[C1:C1 + C2, :], b2.rearrange("(c p) -> c p", p=P)).then_inc(rows_in, DMA)
                    sp.dma_start(rows[C1 + C2:, :], W3.rearrange("(c p) o -> c (p o)", p=P)).then_inc(rows_in, DMA)
            sp.wait_ge(w1_zero, 1)
            for row, k, n in w1_runs:
                sp.dma_start(w1_pair[k % P:k % P + n, k // P, :], W1[row:row + n, :]).then_inc(w1_pair_in, DMA)
            for t in range(T):
                s = slice(t * P, (t + 1) * P)
                sp.wait_ge(y_ready, t + 1)
                sp.dma_start(out[s, :].rearrange("b o -> o b"), y[:, s]).then_inc(y_out, DMA)
            sp.wait_ge(y_out, DMA * T)

        @block.gpsimd
        def _(pool):
            pool.memset(ident[:], 0.0).then_inc(ident_zero, 1)
            pool.wait_ge(ident_zero, 1)
            pool.affine_select(out=ident[:], in_=ident[:], compare_op=ALU.not_equal, fill=1.0, base=0,
                               pattern=[[-1, P]], channel_multiplier=1).then_inc(ident_ready, 1)
            for i, n in enumerate((HK, LK)):
                pool.iota(minus_row[:, i:i + 1], [[0, 1]], base=0, channel_multiplier=-n,
                          allow_small_or_imprecise_dtypes=True).then_inc(minus_row_ready, 1)
            pool.memset(w1_pair[:], 0.0).then_inc(w1_zero, 1)
            pool.wait_ge(first_ids_in, DMA)
            for t in range(T):
                if t == 1:
                    pool.wait_ge(other_ids_in, DMA)
                for v in sum(groups_at[t], [])[1:]:
                    f = v - 1
                    if t >= 2:
                        pool.wait_ge(turned, (t - 2) * NG + group_of[v] + 1)
                    pool.indirect_dma_start(emb[:, t % 2, f, :], None, tables[f],
                                            bass.IndirectOffsetOnAxis(idx[:, t, f:f + 1], 0)
                                            ).then_inc(gathered[t % 2][f], DMA)

        @block.tensor
        def _(pe):
            def spread_ids(h):
                pe.wait_ge(hot_ids_ready, 1 if h == 0 else 2)
                if h == 0:
                    pe.wait_ge(ident16_ready, 1)
                else:
                    pe.wait_ge(ids_copied, h)
                for t in range(T):
                    last = pe.matmul(ids_ps[:, t, :], hot_ids[:, h, t:t + 1].to_broadcast([P, P]), ident16[:],
                                     start=True, stop=True)
                last.then_inc(ids_spread, 1)

            def pick(h):
                pe.wait_ge(hot_in[h], DMA)
                if h >= 2:
                    pe.wait_ge(vt_hot, h - 1)
                acc = hot_ps[:, h % 2].rearrange("d t b -> d (t b)")
                for part in range(2):
                    if part == 0:
                        wait_high(pe, h)
                    else:
                        pe.wait_ge(low_ready, h + 1)
                    for k in range(HK):
                        w = [high, low][part][:, h % 2, k * D:(k + 1) * D]
                        if part == 0:
                            pe.wait_ge(onehot_ready, h * HK + k + 1)
                        last = pe.matmul(acc, w, onehot[0:HOT_P, h % 2, k, :],
                                         start=(part == 0 and k == 0), stop=(part == 1 and k == HK - 1))
                last.then_inc(picked, 1)

            def pick_late():
                pe.wait_ge(zt_copied, NR * (TL - 1) + 2)
                wait_high(pe, NH)
                pe.wait_ge(low_ready, NH + 1)
                pe.wait_ge(late_onehot_ready, 1)
                for part in range(2):
                    for k in range(LK):
                        last = pe.matmul(late_ps, [high, low][part][:, NH % 2, k * D:(k + 1) * D],
                                         late_onehot[0:HOT_P, k, :],
                                         start=(part == 0 and k == 0), stop=(part == 1 and k == LK - 1))
                last.then_inc(late_picked, 1)

            def turn(t, q):
                i = t * NG + q
                if i >= 2:
                    pe.wait_ge([vt_act, vt_dve][q % 2], i // 2)
                for at, v in enumerate(groups_at[t][q]):
                    if v == 0:
                        pe.wait_ge(dense_in, DMA)
                        rows_of = dense_sb[:, t, :]
                    else:
                        pe.wait_ge(gathered[t % 2][v - 1], DMA * (t // 2 + 1))
                        rows_of = emb[:, t % 2, v - 1, :]
                    last = pe.transpose(turn_ps[:, q % 2, at, :], rows_of, ident[:])
                last.then_inc(turned, 1)

            def gram(t):
                if t == 0:
                    pe.wait_ge(vt_hot, NH)
                    pe.wait_ge(psum_zero, 1)
                else:
                    pe.wait_ge(z_ready, NR * t)
                if t >= TL:
                    pe.wait_ge(vt_late, 1)
                pe.wait_ge(vt_act, (t + 1) * NG // 2)
                pe.wait_ge(vt_dve, (t + 1) * NG // 2)
                for g in range(Q):
                    for j in range(NQ):
                        v = VT[:, t * P + j * Q + g, :]
                        c = (g % GB) * NV
                        last = pe.matmul(gram_ps[j * Q:j * Q + NV, g // GB, c:c + NV], v, v,
                                         start=True, stop=True, tile_position=(0, j * Q))
                last.then_inc(gram_done, 1)

            def keep_busy(n):
                for _ in range(n):
                    pe.matmul(h2_own[:, 0, :], ident[:], ident[:], start=True, stop=True)

            def layer1_dense(t, half):
                if t == 0:
                    pe.wait_ge(w1_sum_ready, 1)
                    pe.wait_ge(vt_hot, NH)
                else:
                    pe.wait_ge(h1_act, CH * t)
                    pe.wait_ge(h1_dve, CH * t)
                pe.wait_ge(denseT_ready, t + 1)
                for o in range(half * CH, (half + 1) * CH):
                    pe.matmul(h1_ps[:, o // CH, o % CH, :], w1_sum[:, o * P:(o + 1) * P],
                              denseT[:, t * P:(t + 1) * P], start=(o % CH == 0), stop=False, skip_group_check=True)

            def turn_pairs(t, r):
                if r == 0:
                    if t == 0:
                        pe.wait_ge(cols_ready, 1)
                    else:
                        pe.wait_ge(y_ready, t)
                if r == 1:
                    if t == 0:
                        pe.wait_ge(ids_copied, NH + 1)
                    else:
                        pe.wait_ge(h2_dve, t)
                if r == 2:
                    pe.wait_ge(pad_zero, 1)
                    pe.wait_ge(zt_copied, NR * t + 1)
                pe.wait_ge(packed_ready, NR * t + r + 1)
                pe.transpose(chunk_ps[r], packed[:, r * P:(r + 1) * P], ident[:]).then_inc(zt_done, 1)

            def layer1_pairs(t, r):
                if t == 0:
                    pe.wait_ge(w1_pair_in, DMA * len(w1_runs))
                pe.wait_ge(zt_copied, NR * t + r + 1)
                for o in range(C1):
                    last = pe.matmul(h1_ps[:, o // CH, o % CH, :], w1_pair[:, r, o * P:(o + 1) * P], ZT[:, r, :],
                                     start=False, stop=(r == NR - 1), skip_group_check=True)
                    if r == NR - 1 and o % CH == CH - 1:
                        last.then_inc(h1_done, 1)

            def layer2(t):
                if t == 0:
                    pe.wait_ge(w2_in, DMA)
                if t == TL - 1:
                    pe.wait_ge(vt_late, 1)
                for k in range(C1):
                    pe.wait_ge([h1_act, h1_dve][k // CH], CH * t + k % CH + 1)
                    for o in range(C2):
                        last = pe.matmul(h2_ps[o], w2[:, k, o * P:(o + 1) * P], h1[:, k, :],
                                         start=(k == 0), stop=(k == C1 - 1))
                last.then_inc(h2_done, 1)

            def layer3(t):
                for k in range(C2):
                    pe.wait_ge([h2_act, h2_dve][k], t + 1)
                    last = pe.matmul(y_ps, cols[:, C1 + C2 + k:C1 + C2 + k + 1], h2[:, k, :],
                                     start=(k == 0), stop=(k == C2 - 1))
                last.then_inc(y_done, 1)

            pe.wait_ge(ident_ready, 1)
            spread_ids(0)
            for h in range(NH):
                spread_ids(h + 1)
                pick(h)
                if h >= 2:
                    turn(0, h - 2)
                if h == 0:
                    pe.wait_ge(rows_in, 3 * DMA)
                    pe.transpose(zt_ps[:, 0, 0:C1 + 2 * C2], rows[:], ident[0:C1 + 2 * C2, 0:C1 + 2 * C2]
                                 ).then_inc(rows_turned, 1)
            for q in range(NH - 2, NG):
                turn(0, q)
            for t in range(T - 1):
                gram(t)
                turn(t + 1, 0)
                layer1_dense(t, 0)
                turn_pairs(t, 0)
                turn(t + 1, 1)
                turn_pairs(t, 1)
                layer1_dense(t, 1)
                layer1_pairs(t, 0)
                turn_pairs(t, 2)
                if t < T - 2:
                    turn(t + 1, 2)
                layer1_pairs(t, 1)
                if t == TL - 1:
                    pick_late()
                layer1_pairs(t, 2)
                if t < T - 2:
                    turn(t + 1, 3)
                    layer2(t)
                    for q in range(4, NG):
                        turn(t + 1, q)
                    layer3(t)
                else:
                    turn(t + 1, 2)
                    layer2(t)
                    layer3(t)
                    for q in range(3, NG - 1):
                        turn(t + 1, q)
            t = T - 1
            layer1_dense(t, 0)
            layer1_dense(t, 1)
            turn(t, NG - 1)
            pe.wait_ge(h2_dve, T - 1)
            keep_busy(BUSY_TURN)
            gram(t)
            keep_busy(BUSY_SQUARE)
            turn_pairs(t, 0)
            turn_pairs(t, 1)
            layer1_pairs(t, 0)
            turn_pairs(t, 2)
            layer1_pairs(t, 1)
            layer1_pairs(t, 2)
            layer2(t)
            layer3(t)

        @block.scalar
        def _(act):
            def copy_ids(h):
                act.wait_ge(ids_spread, h + 1)
                if h >= 2:
                    act.wait_ge(onehot_ready, (h - 1) * HK)
                act.activation(ids_all[:, h % 2, :], ids_ps[:].rearrange("p t b -> p (t b)"), ACT.Identity,
                               bias=minus_row[:, h // NH:h // NH + 1]).then_inc(ids_copied, 1)

            def round_high(h):
                act.wait_ge(hot_in[h], DMA)
                if h >= 2:
                    act.wait_ge(picked, h - 1)
                act.copy(high[:, h % 2, 0:rows_on[h] * D], hot_tab[:, h % TABS, 0:rows_on[h] * D]).then_inc(high_ready, 1)

            def copy_picked(h):
                act.wait_ge(picked, h + 1)
                act.copy(VT[:, :, HOT[h] + 1], hot_ps[:, h % 2].rearrange("d t b -> d (t b)")).then_inc(vt_hot, 1)

            def copy_late():
                act.wait_ge(late_picked, 1)
                act.copy(VT[:, late, LATE + 1], late_ps).then_inc(vt_late, 1)

            def copy_turned(t, q):
                act.wait_ge(turned, t * NG + q + 1)
                if q == 0:
                    act.copy(denseT[:, t * P:(t + 1) * P], turn_ps[:, 0, 0, :]).then_inc(denseT_ready, 1)
                vt_copies(act.copy, t, q).then_inc(vt_act, 1)

            def copy_pairs(t, r):
                act.wait_ge(zt_done, NR * t + r + 1)
                if t >= 1:
                    act.wait_ge(h1_done, 2 * t)
                act.copy(ZT[:, r, :], chunk_ps[r]).then_inc(zt_copied, 1)

            def relu1(t):
                act.wait_ge(h1_done, 2 * t + 1)
                if t == 0:
                    act.wait_ge(cols_ready, 1)
                else:
                    act.wait_ge(h2_done, t)
                for o in range(CH):
                    act.activation(h1[:, o, :], h1_ps[:, 0, o, :], ACT.Relu, bias=cols[:, o:o + 1]
                                   ).then_inc(h1_act, 1)

            def relu2(t):
                act.wait_ge(h2_done, t + 1)
                if t >= 1:
                    act.wait_ge(y_done, t)
                act.activation(h2[:, 0, :], h2_ps[0], ACT.Relu, bias=cols[:, C1:C1 + 1]).then_inc(h2_act, 1)

            def copy_y(t):
                act.wait_ge(y_done, t + 1)
                act.copy(y[:, t * P:(t + 1) * P], y_ps).then_inc(y_ready, 1)

            act.wait_ge(minus_row_ready, 2)
            act.activation(warm_up[:], minus_row[:, 0:1], ACT.Relu)
            copy_ids(0)
            for h in range(NH):
                copy_ids(h + 1)
                round_high(h + 1)
                if h == 1:
                    act.dma_start(w1_dense[:, 0, :], W1[0:D, :]).then_inc(w1_dense_in, DMA)
                    act.dma_start(w1_dense[:, 1, :], W1[D + NPAIR:, :]).then_inc(w1_dense_in, DMA)
                    act.dma_start(w2[:], W2.rearrange("(c p) o -> p c o", p=P)).then_inc(w2_in, DMA)
                copy_picked(h)
                if h >= 2 and h % 2 == 0:
                    copy_turned(0, h - 2)
            for q in range(NH - 2 + NH % 2, NG, 2):
                copy_turned(0, q)
            for t in range(T - 1):
                copy_turned(t + 1, 0)
                for r in range(NR):
                    copy_pairs(t, r)
                if t < T - 2:
                    copy_turned(t + 1, 2)
                if t == TL - 1:
                    copy_late()
                relu1(t)
                if t == T - 2:
                    copy_turned(t + 1, 2)
                relu2(t)
                if t < T - 2:
                    copy_turned(t + 1, 4)
                copy_y(t)
                if t == T - 2:
                    copy_turned(t + 1, 4)
            t = T - 1
            for r in range(NR):
                copy_pairs(t, r)
            relu1(t)
            relu2(t)
            copy_y(t)

        @block.vector
        def _(dve):
            def split(h):
                if h >= 2:
                    dve.wait_ge(picked, h - 1)
                dve.wait_ge(ids_copied, h + 1)
                for k in range(HK):
                    dve.tensor_scalar(onehot[:, h % 2, k, :], ids_all[:, h % 2, :], float(k), None,
                                      ALU.is_equal).then_inc(onehot_ready, 1)
                lower(h)

            def lower(h):
                w = slice(0, rows_on[h] * D)
                if h == NH:
                    dve.wait_ge(picked, h - 1)
                wait_high(dve, h)
                dve.tensor_tensor(low[:, h % 2, w], hot_tab[:, h % TABS, w], high[:, h % 2, w].bitcast(F32),
                                  ALU.subtract).then_inc(low_ready, 1)

            def late_onehots():
                dve.wait_ge(ids_copied, NH + 1)
                for k in range(LK):
                    last = dve.tensor_scalar(late_onehot[:, k, :], ids_all[:, NH % 2, late], float(k), None,
                                             ALU.is_equal)
                last.then_inc(late_onehot_ready, 1)

            def copy_turned(t, q):
                dve.wait_ge(turned, t * NG + q + 1)
                vt_copies(dve.tensor_copy, t, q).then_inc(vt_dve, 1)

            def square(t):
                dve.wait_ge(gram_done, t + 1)
                src = gram_ps[:, :, 0:GB * NV].rearrange("p h (g a) -> p a h g", a=NV)
                for r in range(NR):
                    a0, a1 = rects_of[r][0][0], rects_of[r][-1][1]
                    dve.transpose(Z[:, a0:a1, :], src[:, a0:a1]).then_inc(z_ready, 1)
                    dve.wait_ge(z_ready, NR * t + r + 1)
                    if t >= 1:
                        dve.wait_ge(zt_done, NR * t)
                    for a0, a1, place in rects_of[r]:
                        w = NV - 1 - a0
                        dst = packed[:, place:place + (a1 - a0) * w].rearrange("p (a n) -> p a n", n=w)
                        last = dve.tensor_copy(dst, Z[:, a0:a1, a0 + 1:NV])
                    last.then_inc(packed_ready, 1)

            def relu1(t):
                if t >= 1:
                    dve.wait_ge(h2_done, t)
                dve.wait_ge(h1_done, 2 * t + 2)
                for o in range(CH, C1):
                    dve.tensor_scalar(h1[:, o, :], h1_ps[:, 1, o - CH, :], cols[:, o:o + 1], 0.0, ALU.add, ALU.max
                                      ).then_inc(h1_dve, 1)

            def relu2(t):
                dve.wait_ge(h2_done, t + 1)
                if t >= 1:
                    dve.wait_ge(y_done, t)
                dve.tensor_scalar(h2[:, 1, :], h2_ps[1], cols[:, C1 + 1:C1 + 2], 0.0, ALU.add, ALU.max
                                  ).then_inc(h2_dve, 1)

            dve.memset(gram_ps[:], 0.0).then_inc(psum_zero, 1)
            dve.wait_ge(ident_ready, 1)
            dve.tensor_copy(ident16[:], ident[:]).then_inc(ident16_ready, 1)
            dve.wait_ge(first_ids_in, DMA)
            dve.wait_ge(other_ids_in, DMA)
            for h, f in enumerate(HOT + (LATE,)):
                last = dve.tensor_copy(hot_ids[:, h, :], idx[:, :, f])
                if h == 0 or h == NH:
                    last.then_inc(hot_ids_ready, 1)
            dve.memset(packed[:, NZ:], 0.0).then_inc(pad_zero, 1)
            dve.wait_ge(hot_in[0], DMA)
            dve.tensor_copy(high[:, 0, 0:HK * D], hot_tab[:, 0, 0:HK * D]).then_inc(first_high_ready, 1)
            for h in range(NH):
                split(h)
                if h >= 4 and h % 2 == 0:
                    copy_turned(0, h - 3)
                if h == 2:
                    dve.wait_ge(rows_turned, 1)
                    dve.tensor_copy(cols[:], zt_ps[:, 0, 0:C1 + 2 * C2]).then_inc(cols_ready, 1)
            for q in range(NH - 3 | 1, NG, 2):
                copy_turned(0, q)
            dve.wait_ge(w1_dense_in, 2 * DMA)
            dve.tensor_tensor(w1_sum[:], w1_dense[:, 0, :], w1_dense[:, 1, :], ALU.add).then_inc(w1_sum_ready, 1)
            lower(NH)
            for t in range(T - 1):
                if t == TL - 1:
                    late_onehots()
                square(t)
                copy_turned(t + 1, 1)
                relu1(t)
                if t < T - 2:
                    copy_turned(t + 1, 3)
                relu2(t)
                for q in range(5 if t < T - 2 else 3, NG, 2):
                    copy_turned(t + 1, q)
            t = T - 1
            square(t)
            relu1(t)
            relu2(t)


NF_IN = 26
_INS = ["r_dense_proj", "ids"] + [f"tbl_{f}" for f in range(NF_IN)] + ["W_top1", "b_top1", "W_top2", "b_top2", "W_top3"]


def kernel(**inputs):
    import numpy as np
    import concourse.bacc as bacc
    from concourse.bass_utils import run_bass_kernel_spmd

    nc = bacc.Bacc("TRN2", target_bir_lowering=False, num_devices=1)
    arrays, args = {}, []
    for name in _INS:
        a = np.ascontiguousarray(inputs[name])
        dt = U32 if name == "ids" else mybir.dt.from_np(a.dtype)
        arrays[f"in_{name}"] = a
        args.append(nc.dram_tensor(f"in_{name}", a.shape, dt, kind="ExternalInput").ap())
    B = inputs["ids"].shape[0]
    out = nc.dram_tensor("out_y", (B, 1), F32, kind="ExternalOutput").ap()
    dense, ids, tables, top = args[0], args[1], args[2:2 + NF_IN], args[2 + NF_IN:]
    build(nc, dense, ids, tables, *top, out)
    return run_bass_kernel_spmd(nc, [arrays], core_ids=[0]).results[0]["out_y"]
```
